# Optimizing a Trainium2 kernel written in Bass

```python
import numpy as np
import jax
import jax.numpy as jnp

def _softmax(x, axis=-1):
    return jax.nn.softmax(x, axis=axis)

def _gelu(x):
    return jax.nn.gelu(x, approximate=True)

def _silu(x):
    return jax.nn.silu(x)

def _sigmoid(x):
    return jax.nn.sigmoid(x)

def _layernorm(x, axis=-1, eps=1e-05):
    m = jnp.mean(x, axis=axis, keepdims=True)
    v = jnp.var(x, axis=axis, keepdims=True)
    return (x - m) / jnp.sqrt(v + eps)

def _scatter_add(tgt, idx, src, axis=0):
    return tgt.at[idx].add(src)

def _segment_sum(src, seg, n):
    return jax.ops.segment_sum(src, seg, n)
kernel_name = 'mk_gnn_preln_d4_gnn_r8_91006c'

def setup_inputs(seed: int=0):
    np.random.seed(seed)
    _w = jnp.asarray

    def _rec_inputs():
        import jax
        import jax.numpy as jnp
        _gk = jax.random.key(seed)
        x = -0.000202 + 1 * jax.random.normal(jax.random.fold_in(_gk, 1), (12500, 64), jnp.float32)
        _s = jax.random.randint(jax.random.fold_in(_gk, 2), (100000,), 0, 12500, jnp.int32)
        _d = jax.random.randint(jax.random.fold_in(_gk, 3), (100000,), 0, 12500, jnp.int32)
        _loop = jnp.arange(12500, dtype=jnp.int32)
        src = jnp.concatenate([_s, _d, _loop])
        dst = jnp.concatenate([_d, _s, _loop])
        _o = jnp.argsort(dst, stable=True)
        src = src[_o]
        dst = dst[_o]
        edge_attr_64 = -8.16379e-05 + 0.999858 * jax.random.normal(jax.random.fold_in(_gk, 12), (212500, 64), jnp.float32)
        edge_type_8 = jax.random.randint(jax.random.fold_in(_gk, 14), (212500,), 0, 8, jnp.int32)
        return (x, src, dst, edge_attr_64, edge_type_8)
    x, src, dst, edge_attr_64, edge_type_8 = _rec_inputs()

    def _L0_gnn_setup():
        import jax, jax.numpy as jnp
        import numpy as np
        N = 12500
        E = 200000
        D = 64
        H = 128
        OUT = 64
        EPS = 1e-07
        BN_EPS = 1e-05
        NORM_EPS = 1e-12
        key = jax.random.key(seed)
        ks = jax.random.split(key, 10)
        feats = jax.random.normal(ks[0], (N, D), dtype=jnp.float32)
        edge_h = jax.random.normal(ks[1], (E, D), dtype=jnp.float32)
        src = jax.random.randint(ks[2], (E,), 0, N, dtype=jnp.int32)
        dst = jax.random.randint(ks[3], (E,), 0, N, dtype=jnp.int32)
        W1 = jax.random.normal(ks[4], (D, H), dtype=jnp.float32) * 0.05
        b1 = jnp.zeros((H,), dtype=jnp.float32)
        gamma = jnp.ones((H,), dtype=jnp.float32)
        bn_beta = jnp.zeros((H,), dtype=jnp.float32)
        W2 = jax.random.normal(ks[5], (H, OUT), dtype=jnp.float32) * 0.05
        b2 = jnp.zeros((OUT,), dtype=jnp.float32)
        scale = jnp.ones((1,), dtype=jnp.float32)
        return {'feats': feats, 'edge_h': edge_h, 'src': src, 'dst': dst, 'W1': W1, 'b1': b1, 'gamma': gamma, 'bn_beta': bn_beta, 'W2': W2, 'b2': b2, 'scale': scale}
    _L0_gnn_all = _L0_gnn_setup()
    _L0_gnn_in = {k: v for k, v in _L0_gnn_all.items() if k in ('W1', 'b1', 'gamma', 'bn_beta', 'W2', 'b2', 'scale')}
    del _L0_gnn_all

    def _L1_gnn_setup():
        import jax, jax.numpy as jnp
        import numpy as np
        N_NODES = 12500
        N_EDGES = 200000
        F_IN = 64
        F_OUT = 64
        key = jax.random.key(seed)
        k1, k2, k3, k4 = jax.random.split(key, 4)
        x = jax.random.normal(k1, (N_NODES, F_IN), dtype=jnp.float32)
        edge_index = jax.random.randint(k2, (2, N_EDGES), 0, N_NODES, dtype=jnp.int64)
        lim = 1.0 / np.sqrt(2 * F_IN)
        W = jax.random.uniform(k3, (F_OUT, 2 * F_IN), minval=-lim, maxval=lim, dtype=jnp.float32)
        b = jax.random.uniform(k4, (F_OUT,), minval=-lim, maxval=lim, dtype=jnp.float32)
        return {'x': x, 'edge_index': edge_index, 'num_nodes': N_NODES, 'W': W, 'b': b}
    _L1_gnn_all = _L1_gnn_setup()
    _L1_gnn_in = {k: v for k, v in _L1_gnn_all.items() if k in ('W', 'b')}
    del _L1_gnn_all

    def _L2_gnn_setup():
        import jax, jax.numpy as jnp
        import numpy as np
        EPS = 1e-15
        CLIP = 0.98
        N_NODES = 12500
        N_EDGES = 200000
        D_IN = 64
        D_OUT = 64

        def _norm(x):
            return jnp.sqrt(jnp.sum(x * x, axis=1, keepdims=True))

        def _forward(h, W, c, edge_index):
            N = h.shape[0]
            f = h + EPS
            f = f * CLIP / jnp.maximum(CLIP, _norm(f))
            fn = _norm(f)
            p = jnp.tanh(fn) * f / fn
            sqrt_c = jnp.sqrt(c)
            p = p + EPS
            p = p * CLIP / jnp.maximum(CLIP, _norm(p))
            Mp = p @ W
            pn = _norm(p)
            atan_norm = jnp.arctanh(jnp.clip(sqrt_c * pn, -0.9, 0.9))
            t = Mp * atan_norm / pn / sqrt_c
            clip2 = CLIP / sqrt_c
            t = t * clip2 / jnp.maximum(clip2, _norm(t))
            tn = _norm(t)
            hh = jnp.tanh(sqrt_c * tn) / sqrt_c / tn * t
            row, col = (edge_index[0], edge_index[1])
            u = -hh[row]
            v = hh[col]
            c0 = c[0]
            sqrt_c0 = jnp.sqrt(c0)
            nu = jnp.sum(u * u, axis=1)
            nv = jnp.sum(v * v, axis=1)
            duv = jnp.sum(u * v, axis=1)
            coef1 = 1.0 + 2.0 * c0 * duv + c0 * nv
            coef2 = 1.0 - c0 * nu
            den = 1.0 + 2.0 * c0 * duv + c0 * c0 * nu * nv
            ma = (coef1[:, None] * u + coef2[:, None] * v) / den[:, None]
            rn = jnp.sqrt(jnp.sum(ma * ma, axis=1))
            e = -2.0 / sqrt_c0 * jnp.arctanh(jnp.clip(sqrt_c0 * rn, 1e-08, CLIP))
            e_max = jax.ops.segment_max(e, row, num_segments=N)
            e_max = jnp.where(jnp.isfinite(e_max), e_max, 0.0)
            ex = jnp.exp(e - e_max[row])
            denom = jax.ops.segment_sum(ex, row, num_segments=N)
            attention = ex / (denom[row] + 1e-16)
            g = hh + EPS
            g = g * CLIP / jnp.maximum(CLIP, _norm(g))
            gn = _norm(g)
            log_h = jnp.arctanh(jnp.clip(sqrt_c * gn, -0.9, 0.9)) * g / gn
            weighted = sqrt_c0 * attention[:, None] * log_h[col]
            att_log_h = jax.ops.segment_sum(weighted, row, num_segments=N)
            z = jax.nn.elu(att_log_h) + EPS
            clip3 = CLIP / sqrt_c
            z = z * clip3 / jnp.maximum(clip3, _norm(z))
            zn = _norm(z)
            h_prime = jnp.tanh(sqrt_c * zn) * z / sqrt_c / zn
            return h_prime
        key = jax.random.key(seed)
        k1, k2, k3 = jax.random.split(key, 3)
        h = jax.random.normal(k1, (N_NODES, D_IN), dtype=jnp.float32)
        limit = 1.414 * np.sqrt(6.0 / (D_IN + D_OUT))
        W = jax.random.uniform(k2, (D_IN, D_OUT), dtype=jnp.float32, minval=-limit, maxval=limit)
        c = jnp.array([1.0], dtype=jnp.float32)
        edge_index = jax.random.randint(k3, (2, N_EDGES), 0, N_NODES, dtype=jnp.int32)
        return {'h': h, 'W': W, 'c': c, 'edge_index': edge_index}
    _L2_gnn_all = _L2_gnn_setup()
    _L2_gnn_in = {k: v for k, v in _L2_gnn_all.items() if k in ('W', 'c')}
    del _L2_gnn_all

    def _L3_gnn_setup():
        import jax, jax.numpy as jnp
        import numpy as np
        N_NODES = 12500
        N_EDGES = 125000
        N_RELS = 8
        N_HEADS = 4
        IN_FEAT = 64
        OUT_FEAT = 64
        D_HEAD = OUT_FEAT // N_HEADS
        LEAKY_SLOPE = 0.2
        key = jax.random.key(seed)
        ks = jax.random.split(key, 8)
        x = jax.random.normal(ks[0], (N_NODES, IN_FEAT), dtype=jnp.float32)
        src_idx = jax.random.randint(ks[1], (N_EDGES,), 0, N_NODES)
        dst_idx = jax.random.randint(ks[2], (N_EDGES,), 0, N_NODES)
        edge_rel = jnp.sort(jax.random.randint(ks[3], (N_EDGES,), 0, N_RELS))
        conv_weights = jax.random.normal(ks[4], (N_RELS, N_HEADS, IN_FEAT, D_HEAD), dtype=jnp.float32) * 0.1
        attn_l = jax.random.normal(ks[5], (N_RELS, N_HEADS, D_HEAD), dtype=jnp.float32) * 0.1
        attn_r = jax.random.normal(ks[6], (N_RELS, N_HEADS, D_HEAD), dtype=jnp.float32) * 0.1
        h_bias = jnp.zeros((OUT_FEAT,), dtype=jnp.float32)
        return {'x': x, 'src_idx': src_idx, 'dst_idx': dst_idx, 'edge_rel': edge_rel, 'conv_weights': conv_weights, 'attn_l': attn_l, 'attn_r': attn_r, 'h_bias': h_bias}
    _L3_gnn_all = _L3_gnn_setup()
    _L3_gnn_in = {k: v for k, v in _L3_gnn_all.items() if k in ('conv_weights', 'attn_l', 'attn_r', 'h_bias')}
    del _L3_gnn_all
    return {'x': x, 'src': src, 'dst': dst, 'edge_attr_64': edge_attr_64, 'edge_type_8': edge_type_8, 'L0_gnn_W1': _L0_gnn_in['W1'], 'L0_gnn_b1': _L0_gnn_in['b1'], 'L0_gnn_gamma': _L0_gnn_in['gamma'], 'L0_gnn_bn_beta': _L0_gnn_in['bn_beta'], 'L0_gnn_W2': _L0_gnn_in['W2'], 'L0_gnn_b2': _L0_gnn_in['b2'], 'L0_gnn_scale': _L0_gnn_in['scale'], 'L1_gnn_W': _L1_gnn_in['W'], 'L1_gnn_b': _L1_gnn_in['b'], 'L2_gnn_W': _L2_gnn_in['W'], 'L2_gnn_c': _L2_gnn_in['c'], 'L3_gnn_conv_weights': _L3_gnn_in['conv_weights'], 'L3_gnn_attn_l': _L3_gnn_in['attn_l'], 'L3_gnn_attn_r': _L3_gnn_in['attn_r'], 'L3_gnn_h_bias': _L3_gnn_in['h_bias']}

def reference(x, src, dst, edge_attr_64, edge_type_8, L0_gnn_W1, L0_gnn_b1, L0_gnn_gamma, L0_gnn_bn_beta, L0_gnn_W2, L0_gnn_b2, L0_gnn_scale, L1_gnn_W, L1_gnn_b, L2_gnn_W, L2_gnn_c, L3_gnn_conv_weights, L3_gnn_attn_l, L3_gnn_attn_r, L3_gnn_h_bias):
    import jax
    import jax.numpy as jnp

    def _L0_gnn_ref(feats, edge_h, W1, b1, gamma, bn_beta, W2, b2, scale, src, dst):
        import jax, jax.numpy as jnp
        import numpy as np
        N = 12500
        E = 200000
        D = 64
        H = 128
        OUT = 64
        EPS = 1e-07
        BN_EPS = 1e-05
        NORM_EPS = 1e-12
        beta = 1.0
        m = jax.nn.relu(feats[src] + edge_h) + EPS
        logits = m * beta
        gmax = jax.ops.segment_max(logits, dst, num_segments=N)
        ex = jnp.exp(logits - gmax[dst])
        den = jax.ops.segment_sum(ex, dst, num_segments=N)
        a = ex / den[dst]
        h = jax.ops.segment_sum(m * a, dst, num_segments=N)
        feat_norm = jnp.linalg.norm(feats, axis=-1, keepdims=True)
        msg_norm = jnp.linalg.norm(h, axis=-1, keepdims=True)
        msg = h / jnp.maximum(msg_norm, NORM_EPS)
        x = feats + msg * feat_norm * scale
        x = x @ W1 + b1
        mean = jnp.mean(x, axis=0)
        var = jnp.mean(jnp.square(x - mean), axis=0)
        x = (x - mean) * jax.lax.rsqrt(var + BN_EPS) * gamma + bn_beta
        x = jax.nn.relu(x)
        return x @ W2 + b2

    def _L1_gnn_ref(x, edge_index, num_nodes, W, b):
        import jax, jax.numpy as jnp
        import numpy as np
        N_NODES = 12500
        N_EDGES = 200000
        F_IN = 64
        F_OUT = 64
        src = edge_index[0]
        dst = edge_index[1]
        agg = jax.ops.segment_sum(x[src], dst, num_segments=num_nodes)
        deg = jax.ops.segment_sum(jnp.ones((edge_index.shape[1],), dtype=x.dtype), dst, num_segments=num_nodes)
        agg = agg / jnp.maximum(deg, 1.0)[:, None]
        h = jnp.concatenate([agg, x], axis=-1)
        out = h @ W.T + b
        return out

    def _L2_gnn_ref(h, W, c, edge_index):
        import jax, jax.numpy as jnp
        import numpy as np
        EPS = 1e-15
        CLIP = 0.98
        N_NODES = 12500
        N_EDGES = 200000
        D_IN = 64
        D_OUT = 64

        def _norm(x):
            return jnp.sqrt(jnp.sum(x * x, axis=1, keepdims=True))

        def _forward(h, W, c, edge_index):
            N = h.shape[0]
            f = h + EPS
            f = f * CLIP / jnp.maximum(CLIP, _norm(f))
            fn = _norm(f)
            p = jnp.tanh(fn) * f / fn
            sqrt_c = jnp.sqrt(c)
            p = p + EPS
            p = p * CLIP / jnp.maximum(CLIP, _norm(p))
            Mp = p @ W
            pn = _norm(p)
            atan_norm = jnp.arctanh(jnp.clip(sqrt_c * pn, -0.9, 0.9))
            t = Mp * atan_norm / pn / sqrt_c
            clip2 = CLIP / sqrt_c
            t = t * clip2 / jnp.maximum(clip2, _norm(t))
            tn = _norm(t)
            hh = jnp.tanh(sqrt_c * tn) / sqrt_c / tn * t
            row, col = (edge_index[0], edge_index[1])
            u = -hh[row]
            v = hh[col]
            c0 = c[0]
            sqrt_c0 = jnp.sqrt(c0)
            nu = jnp.sum(u * u, axis=1)
            nv = jnp.sum(v * v, axis=1)
            duv = jnp.sum(u * v, axis=1)
            coef1 = 1.0 + 2.0 * c0 * duv + c0 * nv
            coef2 = 1.0 - c0 * nu
            den = 1.0 + 2.0 * c0 * duv + c0 * c0 * nu * nv
            ma = (coef1[:, None] * u + coef2[:, None] * v) / den[:, None]
            rn = jnp.sqrt(jnp.sum(ma * ma, axis=1))
            e = -2.0 / sqrt_c0 * jnp.arctanh(jnp.clip(sqrt_c0 * rn, 1e-08, CLIP))
            e_max = jax.ops.segment_max(e, row, num_segments=N)
            e_max = jnp.where(jnp.isfinite(e_max), e_max, 0.0)
            ex = jnp.exp(e - e_max[row])
            denom = jax.ops.segment_sum(ex, row, num_segments=N)
            attention = ex / (denom[row] + 1e-16)
            g = hh + EPS
            g = g * CLIP / jnp.maximum(CLIP, _norm(g))
            gn = _norm(g)
            log_h = jnp.arctanh(jnp.clip(sqrt_c * gn, -0.9, 0.9)) * g / gn
            weighted = sqrt_c0 * attention[:, None] * log_h[col]
            att_log_h = jax.ops.segment_sum(weighted, row, num_segments=N)
            z = jax.nn.elu(att_log_h) + EPS
            clip3 = CLIP / sqrt_c
            z = z * clip3 / jnp.maximum(clip3, _norm(z))
            zn = _norm(z)
            h_prime = jnp.tanh(sqrt_c * zn) * z / sqrt_c / zn
            return h_prime
        return _forward(h, W, c, edge_index)

    def _L3_gnn_ref(x, src_idx, dst_idx, edge_rel, conv_weights, attn_l, attn_r, h_bias):
        import jax, jax.numpy as jnp
        import numpy as np
        N_NODES = 12500
        N_EDGES = 125000
        N_RELS = 8
        N_HEADS = 4
        IN_FEAT = 64
        OUT_FEAT = 64
        D_HEAD = OUT_FEAT // N_HEADS
        LEAKY_SLOPE = 0.2
        N = x.shape[0]
        feat_all = jnp.einsum('ni,rhid->rnhd', x, conv_weights)
        el_all = jnp.einsum('rnhd,rhd->rnh', feat_all, attn_l)
        er_all = jnp.einsum('rnhd,rhd->rnh', feat_all, attn_r)
        feat_e = feat_all[edge_rel, src_idx]
        el = el_all[edge_rel, src_idx]
        er = er_all[edge_rel, dst_idx]
        s = jax.nn.leaky_relu(el + er, negative_slope=LEAKY_SLOPE)
        m = jax.ops.segment_max(s, dst_idx, num_segments=N)
        e = jnp.exp(s - m[dst_idx])
        denom = jax.ops.segment_sum(e, dst_idx, num_segments=N)
        w = e / jnp.maximum(denom[dst_idx], jnp.float32(1e-16))
        agg = jax.ops.segment_sum(feat_e * w[..., None], dst_idx, num_segments=N)
        h = agg.reshape(N, OUT_FEAT) + h_bias
        return h
    edge_index = jnp.stack([src, dst])
    h = jnp.maximum(_layernorm(x, axis=-1), 0.0)
    x = x + _L0_gnn_ref(h, edge_attr_64, L0_gnn_W1, L0_gnn_b1, L0_gnn_gamma, L0_gnn_bn_beta, L0_gnn_W2, L0_gnn_b2, L0_gnn_scale, src, dst)
    h = jnp.maximum(_layernorm(x, axis=-1), 0.0)
    x = x + _L1_gnn_ref(h, edge_index, 12500, L1_gnn_W, L1_gnn_b)
    h = jnp.maximum(_layernorm(x, axis=-1), 0.0)
    x = x + _L2_gnn_ref(h, L2_gnn_W, L2_gnn_c, edge_index)
    h = jnp.maximum(_layernorm(x, axis=-1), 0.0)
    x = x + _L3_gnn_ref(h, src, dst, edge_type_8, L3_gnn_conv_weights, L3_gnn_attn_l, L3_gnn_attn_r, L3_gnn_h_bias)
    return x

_drawn_inputs = setup_inputs


def setup_inputs(seed=0):
    import zlib

    import numpy as np

    out = dict(_drawn_inputs(seed))
    spreads = {'L0_gnn_b1': (0.0, 0.8),
     'L0_gnn_gamma': (1.0, 0.2),
     'L0_gnn_bn_beta': (0.0, 0.1),
     'L0_gnn_b2': (0.0, 0.1),
     'L3_gnn_h_bias': (0.0, 0.1)}
    factors = {'L3_gnn_attn_r': 2.793}
    for name, (base, spread) in spreads.items():
        noise = np.random.default_rng([zlib.crc32(name.encode()), seed]).standard_normal(out[name].shape)
        drawn = base * np.exp(spread * noise) if base else spread * noise
        out[name] = jnp.asarray(drawn.astype(out[name].dtype))
    for name, factor in factors.items():
        out[name] = (out[name] * factor).astype(out[name].dtype)
    return out
```

```python
from contextlib import ExitStack

import concourse.bass as bass
from concourse import mybir

F32 = mybir.dt.float32
BF16 = mybir.dt.bfloat16
I32 = mybir.dt.int32
ALU = mybir.AluOpType
ACT = mybir.ActivationFunctionType
AX = mybir.AxisListType.X

N, E, D, H = 12500, 212500, 64, 128
RELS, HEADS, DH = 8, 4, 16
P = 128
NP, NB = 125, 100
TILES = 4
W = P * TILES
SLOTS = 4
CHUNKS = SLOTS * -(-E // (SLOTS * W))
EP = CHUNKS * W
PER = EP // P
LASTROW = E - (P - 1) * PER
FULL = E // W
TAIL = E - FULL * W
ET = EP // P
FAR = float(1 << 20)
NEG = -1e30
SRC3 = D + HEADS
ROW3 = D + 2 * HEADS
ROW2 = D + 2
ACC2 = D + 1
CLIP = 0.98
EPS2 = 1e-15


def build(nc, x, src, dst, edge_attr, edge_type, w0a, b0a, gamma, beta, w0b, b0b, scale0,
          w1, b1, w2, c2, w3, al3, ar3, b3, out):
    with ExitStack() as whole:
        def dram(name, shape, dt):
            return nc.dram_tensor(name, shape, dt, kind="Internal").ap()

        src_g = dram("src_g", (EP,), I32)
        dst_g = dram("dst_g", (EP,), I32)
        src3 = dram("src3", (EP,), I32)
        dst3 = dram("dst3", (EP,), I32)
        src_f = dram("src_f", (EP,), F32)
        dst_i = dram("dst_i", (EP,), F32)
        same = dram("same", (EP,), BF16)
        part = dram("part", (EP,), BF16)
        starts = dram("starts", (ET,), F32)
        tail = dram("tail", (W, D), F32)
        table0 = dram("table0", (N, D), F32)
        table1 = dram("table1", (N, D), F32)
        table2 = dram("table2", (N, ROW2), F32)
        table3s = dram("table3s", (N * RELS, SRC3), F32)
        table3d = dram("table3d", (N * RELS, HEADS), F32)
        scan0 = dram("scan0", (EP, 2 * D), F32)
        scan1 = dram("scan1", (EP, D), F32)
        scan3 = dram("scan3", (EP, 2 * D), F32)
        acc2 = [dram(f"acc2_{k}", (N, ACC2), F32) for k in range(TILES)]

        def sb(name, shape, dt, ctx=whole):
            return ctx.enter_context(nc.sbuf_tensor(name, shape, dt))

        def counter(names, ctx):
            return [nc.alloc_semaphore(name=n) for n in names.split()]

        ident = sb("ident", [P, P], F32)
        ones_b = sb("ones_b", [1, P], BF16)
        ones_f = sb("ones_f", [1, P], F32)
        lower = sb("lower", [P, P], F32)
        X = sb("X", [NP, NB, D], F32)
        Hn = sb("Hn", [NP, NB, D], F32)
        T = sb("T", [NP, NB, D], F32)
        eps5 = sb("eps5", [NP, 1], F32)
        last_edge = sb("last_edge", [NP, NB], I32)
        has_edge = sb("has_edge", [NP, NB], F32)
        inv_deg = sb("inv_deg", [NP, NB], F32)

        def flat_head(a):
            return a[0:(P - 1) * PER].rearrange("(p n) -> p n", p=P - 1)

        def bc(a, width=D):
            return a[:, :, None].broadcast_to([NP, NB, width])

        def nodes(a):
            return a.rearrange("(p b) f -> p b f", p=NP)

        def edges(a, c):
            return a[bass.ds(c * W, W)].rearrange("(p k) -> p k", k=TILES)

        def row(a, c):
            return a[bass.ds(c * W, W)].rearrange("(a n) -> a n", a=1)

        def edge_rows(a, c):
            return a[bass.ds(c * W, W), :].rearrange("(p k) f -> p k f", k=TILES)

        def stepper(eng, sem):
            count = [0]

            def step(ins):
                count[0] += 1
                ins.then_inc(sem, 1)
                eng.wait_ge(sem, count[0])
            return step

        def layernorm_std(act, small, eps5, var_ready, std_ready):
            act.wait_ge(var_ready, 1)
            nc.scalar.activation(small[:, 1, :], small[:, 1, :], ACT.Sqrt, bias=eps5, scale=1.0 / D).then_inc(std_ready, 1)

        def layernorm_relu(dve, step, small, xin, hout, var_ready, std_ready):
            v = nc.vector
            m, r = small[:, 0, :], small[:, 1, :]
            step(v.reduce_sum(m, xin[:, :, :], AX))
            step(v.tensor_scalar(m, m, 1.0 / D, None, ALU.mult))
            step(v.tensor_tensor(hout[:, :, :], xin[:, :, :], bc(m), ALU.subtract))
            step(v.tensor_tensor(T[:, :, :], hout[:, :, :], hout[:, :, :], ALU.mult))
            step(v.reduce_sum(r, T[:, :, :], AX))
            dve.sem_inc(var_ready, 1)
            dve.wait_ge(std_ready, 1)
            step(v.reciprocal(r, r))
            step(v.tensor_tensor(hout[:, :, :], hout[:, :, :], bc(r), ALU.mult))
            step(v.tensor_scalar(hout[:, :, :], hout[:, :, :], 0.0, None, ALU.max))

        with nc.cleanup_on_exit(), ExitStack() as ctx:
            zeros = sb("zeros", [P, NB * ACC2], F32, ctx)
            srcs = sb("srcs", [P, PER], I32, ctx)
            dsts = sb("dsts", [P, PER], I32, ctx)
            types = sb("types", [P, PER], I32, ctx)
            first_prev = sb("first_prev", [P, 1], I32, ctx)
            clampd = sb("clampd", [P, PER], I32, ctx)
            clamps = sb("clamps", [P, PER], I32, ctx)
            row_s = sb("row_s", [P, PER], I32, ctx)
            row_d = sb("row_d", [P, PER], I32, ctx)
            srcf = sb("srcf", [P, PER], F32, ctx)
            dstf = sb("dstf", [P, PER], F32, ctx)
            samef = sb("samef", [P, PER], F32, ctx)
            sameb = sb("sameb", [P, PER], BF16, ctx)
            partb = sb("partb", [P, PER], BF16, ctx)
            padded, loaded, mask_step, ready, stored, cleared = counter("padded loaded mask_step ready stored cleared", ctx)
            flat = lambda a: a.rearrange("(p n) -> p n", p=P)
            with nc.Block() as block:
                @block.sync
                def _(sp):
                    sp.wait_ge(padded, 5)
                    for tile, a in ((srcs, src), (dsts, dst), (types, edge_type)):
                        sp.dma_start(tile[0:P - 1, :], flat_head(a)).then_inc(loaded, 16)
                        sp.dma_start(tile[P - 1:P, 0:LASTROW], a[(P - 1) * PER:E].rearrange("(a n) -> a n", a=1)).then_inc(loaded, 16)
                    sp.dma_start(first_prev[1:P, :], dst[PER - 1:(P - 1) * PER:PER].rearrange("(n a) -> n a", a=1),
                                 allow_slow_non_contiguous=True).then_inc(loaded, 16)
                    sp.dma_start(X[:, :, :], nodes(x)).then_inc(loaded, 16)
                    sp.wait_ge(ready, 1)
                    for a, tile in ((src_g, clamps), (dst_g, clampd), (src3, row_s), (dst3, row_d),
                                    (src_f, srcf), (dst_i, dstf), (same, sameb), (part, partb)):
                        sp.dma_start(flat(a), tile[:, :]).then_inc(stored, 16)
                    sp.dma_start(starts.rearrange("(p n) -> p n", p=P), dstf[:, 0:PER:P], allow_slow_non_contiguous=True).then_inc(stored, 16)
                    sp.wait_ge(stored, 16 * 9)

                @block.scalar
                def _(act):
                    act.wait_ge(padded, 5)
                    act.dma_start(tail[TAIL:W, :].rearrange("(a r) f -> a (r f)", r=TILES),
                                  zeros[0:(W - TAIL) // TILES, 0:TILES * D]).then_inc(cleared, 16)
                    act.dma_start(tail[0:TAIL, :], edge_attr[FULL * W:E, :]).then_inc(cleared, 16)
                    for k in range(TILES):
                        act.dma_start(acc2[k].rearrange("(p b) f -> p (b f)", p=NP), zeros[0:NP, :]).then_inc(cleared, 16)
                    act.wait_ge(cleared, 16 * (2 + TILES))

                @block.gpsimd
                def _(pool):
                    pool.memset(zeros[:, :], 0.0).then_inc(padded, 1)
                    pool.memset(srcs[:, :], 1 << 20).then_inc(padded, 1)
                    pool.memset(dsts[:, :], 1 << 20).then_inc(padded, 1)
                    pool.memset(types[:, :], 0).then_inc(padded, 1)
                    pool.memset(first_prev[:, :], -1).then_inc(padded, 1)
                    pool.memset(ident[:, :], 0.0).then_inc(mask_step, 1)
                    pool.memset(lower[:, :], 1.0).then_inc(mask_step, 1)
                    pool.wait_ge(mask_step, 2)
                    pool.affine_select(out=ident[:, :], in_=ident[:, :], compare_op=ALU.not_equal, fill=1.0,
                                       base=0, pattern=[[-1, P]], channel_multiplier=1).then_inc(mask_step, 1)
                    pool.affine_select(out=lower[:, :], in_=lower[:, :], compare_op=ALU.is_gt, fill=0.0,
                                       base=0, pattern=[[-1, P]], channel_multiplier=1).then_inc(mask_step, 1)
                    pool.memset(ones_b[:, :], 1.0).then_inc(mask_step, 1)
                    pool.memset(ones_f[:, :], 1.0).then_inc(mask_step, 1)
                    pool.wait_ge(mask_step, 6)

                @block.vector
                def _(dve):
                    chain = nc.alloc_semaphore(name="prep_step")
                    step = stepper(dve, chain)
                    v = nc.vector
                    dve.wait_ge(loaded, 16 * 8)
                    step(v.tensor_copy(srcf[:, :], srcs[:, :]))
                    step(v.tensor_copy(dstf[:, :], dsts[:, :]))
                    step(v.tensor_scalar(clampd[:, :], dstf[:, :], float(N - 1), None, ALU.min))
                    step(v.tensor_scalar(samef[:, :], srcf[:, :], float(N), None, ALU.is_lt))
                    step(v.tensor_tensor(clamps[:, :], srcf[:, :], samef[:, :], ALU.mult))
                    step(v.scalar_tensor_tensor(row_s[:, :], clamps[:, :], float(RELS), types[:, :], ALU.mult, ALU.add))
                    step(v.scalar_tensor_tensor(row_d[:, :], clampd[:, :], float(RELS), types[:, :], ALU.mult, ALU.add))
                    step(v.tensor_tensor(samef[:, 1:PER], dsts[:, 1:PER], dsts[:, 0:PER - 1], ALU.is_equal))
                    step(v.tensor_tensor(samef[:, 0:1], dsts[:, 0:1], first_prev[:, :], ALU.is_equal))
                    step(v.tensor_copy(sameb[:, :], samef[:, :]))
                    step(v.tensor_scalar(partb[:, :], samef[:, :], -NEG, NEG, ALU.mult, ALU.add))
                    dve.sem_inc(ready, 1)

        with nc.cleanup_on_exit(), ExitStack() as ctx:
            start_b = sb("start_b", [NP, ET], F32, ctx)
            hits = sb("hits", [NP, 2, ET], BF16, ctx)
            node_i = sb("node_i", [NP, NB], I32, ctx)
            node_f = sb("node_f", [NP, NB], F32, ctx)
            rows_n = sb("rows_n", [NP, NB], F32, ctx)
            row_i = sb("row_i", [NP, NB], I32, ctx)
            rows_g = sb("rows_g", [NP, NB, P], F32, ctx)
            upto = sb("upto", [NP, NB], F32, ctx)
            before = sb("before", [NP, NB], F32, ctx)
            small = sb("small0", [NP, 2, NB], F32, ctx)
            got_starts, numbered, found, gathered, ran, prev_in, prev_out, normed, put, search, upto_ready, var_ready, std_ready = counter(
                "got_starts numbered found gathered ran prev_in prev_out normed put search upto_ready var_ready std_ready", ctx)
            upto_d = dram("upto_d", (N + 1,), F32)
            zero1 = sb("zero1", [1, 1], F32, ctx)
            (consts,) = counter("consts", ctx)
            with nc.Block() as block:
                @block.scalar
                def _(act):
                    act.wait_ge(consts, 1)
                    layernorm_std(act, small, eps5[:, :], var_ready, std_ready)

                @block.sync
                def _(sp):
                    sp.dma_start(start_b[:, :], starts.rearrange("(a n) -> a n", a=1).broadcast_to([NP, ET])).then_inc(got_starts, 16)
                    sp.wait_ge(upto_ready, 1)
                    sp.dma_start(upto_d[1:N + 1].rearrange("(p b) -> p b", p=NP), upto[:, :]).then_inc(prev_out, 16)
                    sp.dma_start(upto_d[0:1].rearrange("(a b) -> a b", a=1), zero1[:, :]).then_inc(prev_out, 16)
                    sp.wait_ge(prev_out, 32)
                    sp.dma_start(before[:, :], upto_d[0:N].rearrange("(p b) -> p b", p=NP)).then_inc(prev_in, 16)
                    sp.wait_ge(normed, 1)
                    sp.dma_start(nodes(table0), Hn[:, :, :]).then_inc(put, 16)
                    sp.wait_ge(put, 16)
                    sp.wait_ge(prev_in, 16)

                @block.gpsimd
                def _(pool):
                    pool.memset(eps5[:, :], 1e-5).then_inc(consts, 1)
                    pool.wait_ge(consts, 1)
                    pool.iota(node_i[:, :], pattern=[[1, NB]], base=0, channel_multiplier=NB).then_inc(numbered, 1)
                    pool.wait_ge(found, 1)
                    for b in range(NB):
                        pool.indirect_dma_start(out=rows_g[:, b, :], out_offset=None,
                                                in_=dst_i.rearrange("(r n) -> r n", n=P),
                                                in_offset=bass.IndirectOffsetOnAxis(ap=row_i[:, b:b + 1], axis=0)).then_inc(gathered, 16)
                    pool.wait_ge(gathered, 16 * NB)

                @block.vector
                def _(dve):
                    v = nc.vector
                    step = stepper(dve, ran)
                    step(v.memset(zero1[:, :], 0.0))
                    dve.wait_ge(numbered, 1)
                    step(v.tensor_copy(node_f[:, :], node_i[:, :]))
                    dve.wait_ge(got_starts, 16)
                    with dve.Fori(0, NB) as b:
                        v.tensor_scalar(hits[:, 0, :], start_b[:, :], node_f[:, bass.ds(b, 1)], 0.0, ALU.is_le, ALU.add,
                                        accum_out=rows_n[:, bass.ds(b, 1)]).then_inc(search, 1)
                        dve.wait_ge(search, b + 1)
                    step(v.tensor_scalar(row_i[:, :], rows_n[:, :], -1.0, 0.0, ALU.add, ALU.max))
                    dve.sem_inc(found, 1)
                    layernorm_relu(dve, step, small, X, Hn, var_ready, std_ready)
                    dve.sem_inc(normed, 1)
                    dve.wait_ge(gathered, 16 * NB)
                    step(v.tensor_tensor(rows_g[:, :, :], rows_g[:, :, :], bc(node_f, P), ALU.is_le))
                    step(v.reduce_sum(upto[:, :], rows_g[:, :, :], AX))
                    step(v.tensor_copy(node_f[:, :], row_i[:, :]))
                    step(v.scalar_tensor_tensor(upto[:, :], node_f[:, :], float(P), upto[:, :], ALU.mult, ALU.add))
                    dve.sem_inc(upto_ready, 1)
                    step(v.tensor_scalar(last_edge[:, :], upto[:, :], -1.0, 0.0, ALU.add, ALU.max))
                    dve.wait_ge(prev_in, 16)
                    step(v.tensor_tensor(before[:, :], upto[:, :], before[:, :], ALU.subtract))
                    step(v.tensor_scalar(has_edge[:, :], before[:, :], 1.0, None, ALU.min))
                    step(v.tensor_scalar(before[:, :], before[:, :], 1.0, None, ALU.max))
                    step(v.reciprocal(inv_deg[:, :], before[:, :]))

        def steps(eng, *stages):
            deep = -(-(max(lag for lag, _ in stages) + SLOTS) // SLOTS) * SLOTS

            def peeled(those):
                for s in those:
                    for lag, stage in stages:
                        if 0 <= s - lag < CHUNKS:
                            stage(s - lag, (s - lag) % SLOTS, (s - lag) // SLOTS)

            peeled(range(deep))
            with eng.Fori(0, (CHUNKS - deep) // SLOTS) as i:
                for j in range(SLOTS):
                    for lag, stage in stages:
                        c = deep + j - lag
                        stage(i * SLOTS + c, c % SLOTS, i + c // SLOTS)
            peeled(range(CHUNKS, CHUNKS + deep))

        def slot_free(eng, sem, c, each=1, ago=2):
            if not (isinstance(c, int) and c < ago):
                eng.wait_ge(sem, c * each + (1 - ago) * each)

        def softmax_edges(layer):
            rel = layer == 3
            GW = 2 * D + HEADS if rel else D
            SW = HEADS if rel else D
            with nc.cleanup_on_exit(), ExitStack() as ctx:
                def psum(name, shape):
                    return ctx.enter_context(nc.psum_tensor(f"{name}_{layer}", shape, F32))

                def buf(name, shape, dt=F32):
                    return sb(f"{name}_{layer}", shape, dt, ctx)

                def sem(name):
                    return nc.alloc_semaphore(name=f"{name}_{layer}")

                idx = buf("idx", [P, SLOTS, TILES], I32)
                idx_d = buf("idx_d", [P, SLOTS, TILES], I32)
                same_r = buf("same_r", [1, SLOTS, W], BF16)
                part_r = buf("part_r", [1, SLOTS, W], BF16)
                rows = buf("rows", [P, SLOTS, TILES, GW])
                added = buf("added", [P, SLOTS, TILES, SW])
                score_e = buf("score_e", [P, 2, TILES, SW])
                wide = buf("wide", [P, 2, TILES, 2 * D])
                score_t = buf("score_t", [P, 2, W])
                fwd = buf("fwd", [P, 2, W])
                bwd = buf("bwd", [P, 2, W])
                ex = buf("ex", [P, 2, W + 1])
                init = buf("init", [P, 2, 1])
                sums = buf("sums", [P, 2, W])
                out_e = buf("out_e", [P, SLOTS, TILES, 2 * D])
                ps_score = psum("ps_score", [P, W])
                ps_mult = psum("ps_mult", [P, 2, W])
                ps_same = psum("ps_same", [P, 2, W])
                ps_part = psum("ps_part", [P, W])
                ps_out = psum("ps_out", [P, 2, W])
                got_idx, got_mask, got_attr, got_rows, put = ([sem(f"{n}{b}") for b in range(SLOTS)] for n in (
                    "got_idx", "got_mask", "got_attr", "got_rows", "put"))
                seeded, summed_in, scored, widened, turned, masked, moved, fwd_done, ends, diffed, exped, weighed, \
                    summed, back, copied, turn, issue = (sem(n) for n in (
                        "seeded summed_in scored widened turned masked moved fwd_done ends diffed exped weighed "
                        "summed back copied turn issue").split())
                scan_out = scan3 if rel else scan0
                IDX, ROWS = (32, 32 * TILES) if rel else (16, 16 * TILES)

                with nc.Block() as block:
                    @block.sync
                    def _(sp):
                        def load(c, b, r):
                            slot_free(sp, scored, c, ago=SLOTS)
                            sp.sem_inc(issue, 1)
                            sp.dma_start(idx[:, b, :], edges(src3 if rel else src_g, c)).then_inc(got_idx[b], 16)
                            if rel:
                                sp.dma_start(idx_d[:, b, :], edges(dst3, c)).then_inc(got_idx[b], 16)
                            else:
                                last = isinstance(c, int) and c == CHUNKS - 1
                                sp.dma_start(added[:, b, :, :], edge_rows(tail, 0) if last else
                                             edge_rows(edge_attr, c)).then_inc(got_attr[b], 16)
                            slot_free(sp, masked, c, ago=SLOTS)
                            sp.sem_inc(issue, 1)
                            sp.dma_start(same_r[:, b, :], row(same, c)).then_inc(got_mask[b], 16)
                            sp.dma_start(part_r[:, b, :], row(part, c)).then_inc(got_mask[b], 16)

                        def store(c, b, r):
                            sp.wait_ge(copied, c + 1)
                            sp.sem_inc(issue, 1)
                            sp.dma_start(edge_rows(scan_out, c), out_e[:, b, :, :]).then_inc(put[b], 16)

                        steps(sp, (2, load), (6, store))
                        for b in range(SLOTS):
                            sp.wait_ge(put[b], 16 * (CHUNKS // SLOTS))

                    @block.gpsimd
                    def _(pool):
                        def gather(c, b, r):
                            pool.wait_ge(got_idx[b], r * IDX + IDX)
                            slot_free(pool, turned if rel else scored, c, ago=SLOTS)
                            pool.sem_inc(turn, 1)
                            for k in range(TILES):
                                pool.indirect_dma_start(
                                    out=rows[:, b, k, D:GW] if rel else rows[:, b, k, :], out_offset=None,
                                    in_=table3s if rel else table0,
                                    in_offset=bass.IndirectOffsetOnAxis(ap=idx[:, b, k:k + 1], axis=0)) \
                                    .then_inc(got_rows[b], 16)
                                if rel:
                                    pool.indirect_dma_start(
                                        out=added[:, b, k, :], out_offset=None, in_=table3d,
                                        in_offset=bass.IndirectOffsetOnAxis(ap=idx_d[:, b, k:k + 1], axis=0)) \
                                        .then_inc(got_rows[b], 16)
                        steps(pool, (0, gather))

                    @block.vector
                    def _(dve):
                        v = nc.vector
                        v.memset(fwd[:, 1, W - 1:W], NEG if rel else 0.0).then_inc(seeded, 1)
                        v.memset(sums[:, 1, W - 1:W], 0.0).then_inc(seeded, 1)
                        if rel:
                            v.memset(rows[:, :, :, 0:D], 1.0).then_inc(seeded, 1)
                        dve.wait_ge(seeded, 3 if rel else 2)

                        def score(c, b, r):
                            dve.wait_ge(got_rows[b], r * ROWS + ROWS)
                            if not rel:
                                dve.wait_ge(got_attr[b], r * 16 + 16)
                            slot_free(dve, widened, c)
                            v.tensor_tensor(score_e[:, b % 2, :, :], rows[:, b, :, 2 * D:GW] if rel else rows[:, b, :, :],
                                            added[:, b, :, :], ALU.add).then_inc(summed_in, 1)
                            dve.wait_ge(summed_in, c + 1)
                            if rel:
                                v.scalar_tensor_tensor(score_e[:, b % 2, :, :], score_e[:, b % 2, :, :], 0.2, score_e[:, b % 2, :, :],
                                                       ALU.mult, ALU.max).then_inc(scored, 1)
                            else:
                                v.tensor_scalar(score_e[:, b % 2, :, :], score_e[:, b % 2, :, :], 0.0, 1e-7,
                                                ALU.max, ALU.add).then_inc(scored, 1)

                        def maxima(c, b, r):
                            dve.wait_ge(moved, c + 1)
                            dve.wait_ge(masked, c + 1)
                            v.tensor_tensor_scan(out=fwd[:, b % 2, :], data0=ps_part[:, :], data1=score_t[:, b % 2, :],
                                                 initial=fwd[:, 1 - b % 2, W - 1:W], op0=ALU.add, op1=ALU.max) \
                                .then_inc(fwd_done, 1)
                            dve.wait_ge(fwd_done, c + 1)
                            v.tensor_copy(bwd[:, b % 2, W - 1:W], fwd[:, b % 2, W - 1:W]).then_inc(ends, 1)
                            v.tensor_tensor_scan(out=bwd[:, b % 2, W - 2::-1], data0=ps_part[:, W - 1:0:-1],
                                                 data1=fwd[:, b % 2, W - 2::-1], initial=fwd[:, b % 2, W - 1:W],
                                                 op0=ALU.add, op1=ALU.max).then_inc(ends, 1)
                            dve.wait_ge(ends, c * 2 + 2)
                            v.tensor_tensor(ex[:, b % 2, 0:W], score_t[:, b % 2, :], bwd[:, b % 2, :], ALU.subtract) \
                                .then_inc(diffed, 1)
                            v.tensor_scalar(ex[:, b % 2, W:W + 1], fwd[:, 1 - b % 2, W - 1:W], bwd[:, b % 2, 0:1], 0.0,
                                            ALU.subtract, ALU.min).then_inc(diffed, 1)

                        def segment_sums(c, b, r):
                            dve.wait_ge(exped, c + 1)
                            slot_free(dve, summed, c, ago=1)
                            v.tensor_tensor(init[:, b % 2, :], ex[:, b % 2, W:W + 1], sums[:, 1 - b % 2, W - 1:W], ALU.mult) \
                                .then_inc(weighed, 1)
                            lo, mult = (0, ps_mult[:, b % 2, :]) if rel else (D, score_t[D:P, b % 2, :])
                            v.tensor_tensor(ex[lo:P, b % 2, 0:W], ex[lo:P, b % 2, 0:W], mult, ALU.mult).then_inc(weighed, 1)
                            dve.wait_ge(weighed, c * 2 + 2)
                            slot_free(dve, back, c)
                            v.tensor_tensor_scan(out=sums[:, b % 2, :], data0=ps_same[:, b % 2, :], data1=ex[:, b % 2, 0:W],
                                                 initial=init[:, b % 2, :], op0=ALU.mult, op1=ALU.add).then_inc(summed, 1)

                        steps(dve, (0, score), (1, maxima), (2, segment_sums))

                    @block.tensor
                    def _(pe):
                        pe.wait_ge(seeded, 3 if rel else 2)

                        def to_columns(c, b, r):
                            pe.wait_ge(widened, c + 1)
                            slot_free(pe, moved, c, ago=1)
                            if rel:
                                slot_free(pe, weighed, c, each=2)
                            for k in range(TILES):
                                mm = nc.tensor.transpose(ps_score[:, k::TILES], wide[:, b % 2, k, :], ident[:, :])
                            if rel:
                                for k in range(TILES):
                                    mm = nc.tensor.transpose(ps_mult[:, b % 2, k::TILES], rows[:, b, k, 0:2 * D], ident[:, :])
                            mm.then_inc(turned, 1)

                        def masks(c, b, r):
                            pe.wait_ge(got_mask[b], r * 32 + 32)
                            slot_free(pe, summed, c)
                            slot_free(pe, ends, c, each=2, ago=1)
                            nc.tensor.matmul(ps_same[:, b % 2, :], ones_b[:, :], same_r[:, b, :], start=True, stop=True)
                            nc.tensor.matmul(ps_part[:, :], ones_b[:, :], part_r[:, b, :], start=True, stop=True) \
                                .then_inc(masked, 1)

                        def to_rows(c, b, r):
                            pe.wait_ge(summed, c + 1)
                            slot_free(pe, copied, c)
                            for k in range(TILES):
                                mm = nc.tensor.transpose(ps_out[:, b % 2, k * P:(k + 1) * P], sums[:, b % 2, k::TILES], ident[:, :])
                            mm.then_inc(back, 1)

                        steps(pe, (0, to_columns), (0, masks), (2, to_rows))

                    @block.scalar
                    def _(act):
                        def widen(c, b, r):
                            act.wait_ge(scored, c + 1)
                            slot_free(act, turned, c)
                            if rel:
                                for k in range(TILES):
                                    ins = nc.scalar.activation(
                                        wide[:, b % 2, k, :].rearrange("p (t h d) -> p t h d", t=2, h=HEADS),
                                        score_e[:, b % 2, k, None, :, None].broadcast_to([P, 2, HEADS, DH]), ACT.Copy)
                            else:
                                ins = nc.scalar.activation(
                                    wide[:, b % 2, :, :].rearrange("p k (t d) -> p k t d", t=2),
                                    score_e[:, b % 2, :, None, :].broadcast_to([P, TILES, 2, D]), ACT.Copy)
                            ins.then_inc(widened, 1)

                        def move(c, b, r):
                            act.wait_ge(turned, c + 1)
                            slot_free(act, weighed, c, each=2)
                            nc.scalar.activation(score_t[:, b % 2, :], ps_score[:, :], ACT.Copy).then_inc(moved, 1)

                        def exps(c, b, r):
                            act.wait_ge(diffed, c * 2 + 2)
                            nc.scalar.activation(ex[:, b % 2, :], ex[:, b % 2, :], ACT.Exp).then_inc(exped, 1)

                        def copy_out(c, b, r):
                            act.wait_ge(back, c + 1)
                            slot_free(act, put[b], r, each=16, ago=1)
                            nc.scalar.activation(out_e[:, b, :, :].rearrange("p k f -> p (k f)"), ps_out[:, b % 2, :], ACT.Copy) \
                                .then_inc(copied, 1)

                        steps(act, (0, widen), (0, move), (1, exps), (3, copy_out))

        def mean_edges():
            with nc.cleanup_on_exit(), ExitStack() as ctx:
                idx = sb("m_idx", [P, SLOTS, TILES], I32, ctx)
                same_r = sb("m_same_r", [1, SLOTS, W], BF16, ctx)
                rows = sb("m_rows", [P, SLOTS, TILES, D], F32, ctx)
                rows_t = sb("m_rows_t", [D, 2, W], F32, ctx)
                sums = sb("m_sums", [D, 2, W], F32, ctx)
                out_e = sb("m_out_e", [P, SLOTS, TILES, D], F32, ctx)
                ps_rows = ctx.enter_context(nc.psum_tensor("m_ps_rows", [D, 2, W], F32))
                ps_same = ctx.enter_context(nc.psum_tensor("m_ps_same", [D, 2, W], F32))
                ps_out = ctx.enter_context(nc.psum_tensor("m_ps_out", [P, 2, 512], F32))
                got_idx, got_mask, got_rows, put = (counter(f"m_{n}0 m_{n}1 m_{n}2 m_{n}3", ctx) for n in
                                                    ("got_idx", "got_mask", "got_rows", "put"))
                seeded, turned, masked, moved, summed, back, copied, turn, issue, pe_turn = counter(
                    "m_seeded m_turned m_masked m_moved m_summed m_back m_copied m_turn m_issue m_pe_turn", ctx)
                with nc.Block() as block:
                    @block.sync
                    def _(sp):
                        def load(c, b, r):
                            slot_free(sp, turned, c, ago=SLOTS)
                            slot_free(sp, masked, c, ago=SLOTS)
                            sp.sem_inc(issue, 1)
                            sp.dma_start(idx[:, b, :], edges(src_g, c)).then_inc(got_idx[b], 16)
                            sp.dma_start(same_r[:, b, :], row(same, c)).then_inc(got_mask[b], 16)

                        def store(c, b, r):
                            sp.wait_ge(copied, c + 1)
                            sp.sem_inc(issue, 1)
                            sp.dma_start(edge_rows(scan1, c), out_e[:, b, :, :]).then_inc(put[b], 16)

                        steps(sp, (0, load), (4, store))
                        for b in range(SLOTS):
                            sp.wait_ge(put[b], 16 * (CHUNKS // SLOTS))

                    @block.gpsimd
                    def _(pool):
                        def gather(c, b, r):
                            pool.wait_ge(got_idx[b], r * 16 + 16)
                            slot_free(pool, turned, c, ago=SLOTS)
                            pool.sem_inc(turn, 1)
                            for k in range(TILES):
                                pool.indirect_dma_start(
                                    out=rows[:, b, k, :], out_offset=None, in_=table1,
                                    in_offset=bass.IndirectOffsetOnAxis(ap=idx[:, b, k:k + 1], axis=0)) \
                                    .then_inc(got_rows[b], 16)
                        steps(pool, (0, gather))

                    @block.tensor
                    def _(pe):
                        def to_columns(c, b, r):
                            pe.wait_ge(got_rows[b], r * 16 * TILES + 16 * TILES)
                            slot_free(pe, moved, c)
                            pe.sem_inc(pe_turn, 1)
                            for k in range(TILES):
                                mm = nc.tensor.transpose(ps_rows[:, b % 2, k::TILES], rows[:, b, k, :], ident[:, :])
                            mm.then_inc(turned, 1)

                        def masks(c, b, r):
                            pe.wait_ge(got_mask[b], r * 16 + 16)
                            slot_free(pe, summed, c)
                            nc.tensor.matmul(ps_same[:, b % 2, :], ones_b[:, 0:D], same_r[:, b, :], start=True, stop=True) \
                                .then_inc(masked, 1)

                        def to_rows(c, b, r):
                            pe.wait_ge(summed, c + 1)
                            slot_free(pe, copied, c)
                            pe.sem_inc(pe_turn, 1)
                            for k in range(TILES):
                                mm = nc.tensor.transpose(ps_out[:, b % 2, k * D:(k + 1) * D], sums[:, b % 2, k::TILES],
                                                         ident[0:D, 0:D])
                            mm.then_inc(back, 1)

                        steps(pe, (0, to_columns), (0, masks), (1, to_rows))

                    @block.scalar
                    def _(act):
                        def move(c, b, r):
                            act.wait_ge(turned, c + 1)
                            slot_free(act, summed, c)
                            nc.scalar.activation(rows_t[:, b % 2, :], ps_rows[:, b % 2, :], ACT.Copy).then_inc(moved, 1)

                        def copy_out(c, b, r):
                            act.wait_ge(back, c + 1)
                            slot_free(act, put[b], r, each=16, ago=1)
                            nc.scalar.activation(out_e[:, b, :, :].rearrange("p k f -> p (k f)"),
                                                 ps_out[:, b % 2, 0:TILES * D], ACT.Copy).then_inc(copied, 1)

                        steps(act, (0, move), (2, copy_out))

                    @block.vector
                    def _(dve):
                        nc.vector.memset(sums[:, 1, W - 1:W], 0.0).then_inc(seeded, 1)
                        dve.wait_ge(seeded, 1)

                        def segment_sums(c, b, r):
                            dve.wait_ge(moved, c + 1)
                            dve.wait_ge(masked, c + 1)
                            slot_free(dve, summed, c, ago=1)
                            slot_free(dve, back, c)
                            nc.vector.tensor_tensor_scan(out=sums[:, b % 2, :], data0=ps_same[:, b % 2, :],
                                                         data1=rows_t[:, b % 2, :], initial=sums[:, 1 - b % 2, W - 1:W],
                                                         op0=ALU.mult, op1=ALU.add).then_inc(summed, 1)
                        steps(dve, (0, segment_sums))

        def hyperbolic_edges(c_col, inv_sqrt_c):
            with nc.cleanup_on_exit(), ExitStack() as ctx:
                def buf(name, shape, dt=F32):
                    return sb(f"h_{name}", shape, dt, ctx)

                def sem(name):
                    return nc.alloc_semaphore(name=f"h_{name}")

                idx_s = buf("idx_s", [P, SLOTS, TILES], I32)
                idx_d = buf("idx_d", [P, SLOTS, TILES], I32)
                key = buf("key", [P, SLOTS, TILES])
                key_r = buf("key_r", [1, SLOTS, W])
                rows_s = buf("rows_s", [P, SLOTS, TILES, ROW2])
                rows_d = buf("rows_d", [P, SLOTS, TILES, ROW2])
                equal = buf("equal", [P, SLOTS, TILES, P])
                earlier = buf("earlier", [P, TILES, P])
                rank = buf("rank", [P, TILES])
                target = buf("target", [P, SLOTS, TILES], I32)
                diff = buf("diff", [P, TILES, D])
                point = buf("point", [P, TILES, D])
                square = buf("square", [P, TILES, D])
                dist = buf("dist", [P, TILES])
                prod = buf("prod", [P, TILES])
                ratio = buf("ratio", [P, SLOTS, TILES])
                low = buf("low", [P, TILES])
                high = buf("high", [P, TILES])
                factor = buf("factor", [P, TILES])
                message = buf("message", [P, SLOTS, TILES, ACC2])
                sums = buf("sums", [P, SLOTS, TILES, ACC2])
                ps_key = ctx.enter_context(nc.psum_tensor("h_ps_key", [P, 2, W], F32))
                ps_sum = ctx.enter_context(nc.psum_tensor("h_ps_sum", [P, 2, 512], F32))
                got_idx, got_key, got_rows = ([sem(f"{n}{b}") for b in range(SLOTS)] for n in ("got_idx", "got_key", "got_rows"))
                added = [sem(f"added{k}") for k in range(TILES)]
                spread, compared, e_step, targeted, p_step, squared, rooted, weighable, weighed, messaged, multiplied, \
                    copied, turn, issue = (sem(n) for n in (
                        "spread compared e_step targeted p_step squared rooted weighable weighed messaged multiplied "
                        "copied turn issue").split())
                d_step, r_step = sem("d_step"), sem("r_step")
                w_step = sem("w_step")

                with nc.Block() as block:
                    @block.sync
                    def _(sp):
                        def load(c, b, r):
                            slot_free(sp, messaged, c, ago=SLOTS)
                            slot_free(sp, targeted, c, ago=SLOTS)
                            sp.sem_inc(issue, 1)
                            sp.dma_start(idx_s[:, b, :], edges(src_g, c)).then_inc(got_idx[b], 16)
                            sp.dma_start(idx_d[:, b, :], edges(dst_g, c)).then_inc(got_idx[b], 16)
                            sp.dma_start(key[:, b, :], edges(src_f, c)).then_inc(got_key[b], 16)
                            sp.dma_start(key_r[:, b, :], row(src_f, c)).then_inc(got_key[b], 16)
                        steps(sp, (0, load))

                    @block.gpsimd
                    def _(pool):
                        def gather(c, b, r):
                            pool.wait_ge(got_idx[b], r * 32 + 32)
                            slot_free(pool, messaged, c, ago=SLOTS)
                            pool.sem_inc(turn, 1)
                            for k in range(TILES):
                                for rows, idx in ((rows_s, idx_s), (rows_d, idx_d)):
                                    pool.indirect_dma_start(
                                        out=rows[:, b, k, :], out_offset=None, in_=table2,
                                        in_offset=bass.IndirectOffsetOnAxis(ap=idx[:, b, k:k + 1], axis=0)) \
                                        .then_inc(got_rows[b], 16)

                        def add(c, b, r):
                            pool.wait_ge(copied, c + 1)
                            pool.wait_ge(targeted, c + 1)
                            pool.sem_inc(turn, 1)
                            for k in range(TILES):
                                slot_free(pool, added[k], c, each=16, ago=1)
                                pool.sem_inc(turn, 1)
                                pool.indirect_dma_start(
                                    out=acc2[k], out_offset=bass.IndirectOffsetOnAxis(ap=target[:, b, k:k + 1], axis=0),
                                    in_=sums[:, b, k, :], in_offset=None, bounds_check=N - 1, oob_is_err=False,
                                    compute_op=ALU.add).then_inc(added[k], 16)
                        steps(pool, (0, gather), (3, add))
                        for k in range(TILES):
                            pool.wait_ge(added[k], 16 * CHUNKS)

                    @block.tensor
                    def _(pe):
                        def spread_keys(c, b, r):
                            pe.wait_ge(got_key[b], r * 32 + 32)
                            slot_free(pe, compared, c)
                            nc.tensor.matmul(ps_key[:, b % 2, :], ones_f[:, :], key_r[:, b, :], start=True, stop=True) \
                                .then_inc(spread, 1)

                        def sum_equal(c, b, r):
                            pe.wait_ge(messaged, c + 1)
                            pe.wait_ge(compared, c + 1)
                            slot_free(pe, copied, c)
                            for k in range(TILES):
                                mm = nc.tensor.matmul(ps_sum[:, b % 2, k * ACC2:(k + 1) * ACC2], equal[:, b, k, :],
                                                      message[:, b, k, :], start=True, stop=True)
                            mm.then_inc(multiplied, 1)
                        steps(pe, (0, spread_keys), (2, sum_equal))

                    @block.scalar
                    def _(act):
                        def root(c, b, r):
                            act.wait_ge(squared, c + 1)
                            nc.scalar.activation(ratio[:, b, :], ratio[:, b, :], ACT.Sqrt).then_inc(rooted, 1)

                        def weigh(c, b, r):
                            act.wait_ge(weighable, c + 1)
                            nc.scalar.activation(ratio[:, b, :], ratio[:, b, :], ACT.Ln).then_inc(w_step, 1)
                            act.wait_ge(w_step, c + 1)
                            nc.scalar.activation(message[:, b, :, D], ratio[:, b, :], ACT.Exp,
                                                 scale=inv_sqrt_c[:, :]).then_inc(weighed, 1)

                        def copy_out(c, b, r):
                            act.wait_ge(multiplied, c + 1)
                            if not (isinstance(c, int) and c < SLOTS):
                                for k in range(TILES):
                                    act.wait_ge(added[k], c * 16 + 16 - 16 * SLOTS)
                            nc.scalar.activation(sums[:, b, :, :].rearrange("p k f -> p (k f)"),
                                                 ps_sum[:, b % 2, 0:TILES * ACC2], ACT.Copy).then_inc(copied, 1)
                        steps(act, (0, root), (1, weigh), (2, copy_out))

                    @block.vector
                    def _(dve):
                        v = nc.vector

                        def compare(c, b, r):
                            dve.wait_ge(spread, c + 1)
                            dve.wait_ge(got_key[b], r * 32 + 32)
                            slot_free(dve, multiplied, c, ago=SLOTS)
                            for k in range(TILES):
                                ins = v.tensor_scalar(equal[:, b, k, :], ps_key[:, b % 2, k::TILES], key[:, b, k:k + 1], None,
                                                      ALU.is_equal)
                            ins.then_inc(compared, 1)
                            dve.wait_ge(compared, c + 1)
                            v.tensor_tensor(earlier[:, :, :], equal[:, b, :, :],
                                            lower[:, None, :].broadcast_to([P, TILES, P]), ALU.mult).then_inc(e_step, 1)
                            dve.wait_ge(e_step, c * 2 + 1)
                            v.reduce_sum(rank[:, :], earlier[:, :, :], AX).then_inc(e_step, 1)
                            dve.wait_ge(e_step, c * 2 + 2)
                            if not (isinstance(c, int) and c < SLOTS):
                                for k in range(TILES):
                                    dve.wait_ge(added[k], c * 16 + 16 - 16 * SLOTS)
                            v.scalar_tensor_tensor(target[:, b, :], rank[:, :], FAR, key[:, b, :], ALU.mult, ALU.add) \
                                .then_inc(targeted, 1)

                        def chain(sem, c, length):
                            count = [0]

                            def step(ins):
                                count[0] += 1
                                assert count[0] <= length
                                ins.then_inc(sem, 1)
                                dve.wait_ge(sem, c * length + count[0])
                            return step

                        def distances(c, b, r):
                            step = chain(d_step, c, 7)
                            slot_free(dve, squared, c, ago=1)
                            dve.wait_ge(got_rows[b], r * 32 * TILES + 32 * TILES)
                            step(v.tensor_tensor(diff[:, :, :], rows_s[:, b, :, 0:D], rows_d[:, b, :, 0:D], ALU.subtract))
                            step(v.tensor_tensor(square[:, :, :], diff[:, :, :], diff[:, :, :], ALU.mult))
                            step(v.reduce_sum(dist[:, :], square[:, :, :], AX))
                            step(v.tensor_tensor(prod[:, :], rows_s[:, b, :, D], rows_d[:, b, :, D], ALU.mult))
                            step(v.tensor_scalar(dist[:, :], dist[:, :], c_col[:, :], None, ALU.mult))
                            step(v.tensor_tensor(prod[:, :], prod[:, :], dist[:, :], ALU.add))
                            step(v.reciprocal(prod[:, :], prod[:, :]))
                            slot_free(dve, weighed, c, ago=SLOTS)
                            v.tensor_tensor(ratio[:, b, :], dist[:, :], prod[:, :], ALU.mult).then_inc(squared, 1)

                        def ratios(c, b, r):
                            step = chain(r_step, c, 4)
                            slot_free(dve, weighable, c, ago=1)
                            dve.wait_ge(rooted, c + 1)
                            step(v.tensor_scalar(ratio[:, b, :], ratio[:, b, :], 1e-8, CLIP, ALU.max, ALU.min))
                            step(v.tensor_scalar(low[:, :], ratio[:, b, :], 1.0, None, ALU.add))
                            step(v.tensor_scalar(high[:, :], ratio[:, b, :], -1.0, 1.0, ALU.mult, ALU.add))
                            step(v.reciprocal(low[:, :], low[:, :]))
                            slot_free(dve, multiplied, c, ago=SLOTS)
                            v.tensor_tensor(ratio[:, b, :], high[:, :], low[:, :], ALU.mult).then_inc(weighable, 1)

                        def messages(c, b, r):
                            step = chain(p_step, c, 2)
                            slot_free(dve, messaged, c, ago=1)
                            dve.wait_ge(weighed, c + 1)
                            step(v.tensor_tensor(factor[:, :], message[:, b, :, D], rows_d[:, b, :, D + 1], ALU.mult))
                            step(v.tensor_scalar(point[:, :, :], rows_d[:, b, :, 0:D], EPS2, None, ALU.add))
                            v.tensor_tensor(message[:, b, :, 0:D], point[:, :, :],
                                            factor[:, :, None].broadcast_to([P, TILES, D]), ALU.mult).then_inc(messaged, 1)

                        steps(dve, (0, compare), (0, distances), (1, ratios), (2, messages))


        def gather_last(pool, into, table, sem):
            for b in range(NB):
                pool.indirect_dma_start(out=into[:, b, :], out_offset=None, in_=table,
                                        in_offset=bass.IndirectOffsetOnAxis(ap=last_edge[:, b:b + 1], axis=0)).then_inc(sem, 16)

        GROUP = 4
        GROUPS = NB // GROUP

        class Linear:
            def __init__(self, ctx, name, K, M, banks_of=None):
                self.K, self.M = K, M
                self.banks = -(-GROUP * M // 512)
                self.wide = self.banks > 1
                self.n = NB if self.wide else GROUPS
                self.per = 1 if self.wide else GROUP
                if banks_of:
                    self.ps_t, self.ps_y = banks_of.ps_t[0:K, :, :], banks_of.ps_y
                else:
                    self.ps_t = ctx.enter_context(nc.psum_tensor(f"{name}_ps_t", [K, 2, 512], F32))
                    self.ps_y = ctx.enter_context(nc.psum_tensor(f"{name}_ps_y", [NP, 2, 2 if self.wide else 1, 512], F32))
                self.rows_t = sb(f"{name}_rows_t", [K, 2, GROUP, NP], F32, ctx)
                self.turned, self.moved, self.multiplied, self.taken = counter(
                    f"{name}_turned {name}_moved {name}_multiplied {name}_taken", ctx)

            def pe(self, pe, rows, weights):
                for g in range(self.n + 1):
                    if g < self.n:
                        if g >= 2:
                            pe.wait_ge(self.moved, g - 1)
                        for k in range(self.per):
                            mm = nc.tensor.transpose(self.ps_t[:, g % 2, k * NP:(k + 1) * NP], rows[:, g * self.per + k, :],
                                                     ident[0:NP, 0:NP])
                        mm.then_inc(self.turned, 1)
                    if g >= 1:
                        h = g - 1
                        pe.wait_ge(self.moved, h + 1)
                        if h >= 2:
                            pe.wait_ge(self.taken, h - 1)
                        for k in range(self.per):
                            if self.wide:
                                for half in range(2):
                                    mm = nc.tensor.matmul(self.ps_y[:, h % 2, half, 0:self.M // 2], self.rows_t[:, h % 2, k, :],
                                                          weights[:, half * self.M // 2:(half + 1) * self.M // 2],
                                                          start=True, stop=True)
                            else:
                                mm = nc.tensor.matmul(self.ps_y[:, h % 2, 0, k * self.M:(k + 1) * self.M],
                                                      self.rows_t[:, h % 2, k, :], weights, start=True, stop=True)
                        mm.then_inc(self.multiplied, 1)

            def act(self, act):
                for g in range(self.n):
                    act.wait_ge(self.turned, g + 1)
                    if g >= 2:
                        act.wait_ge(self.multiplied, g - 1)
                    nc.scalar.activation(self.rows_t[:, g % 2, 0:self.per, :].rearrange("p k n -> p (k n)"),
                                         self.ps_t[:, g % 2, 0:self.per * NP], ACT.Copy).then_inc(self.moved, 1)

            def take(self, dve, use):
                for g in range(self.n):
                    dve.wait_ge(self.multiplied, g + 1)
                    use(g, self.ps_y[:, g % 2, :, :]).then_inc(self.taken, 1)

        def col(a):
            return a.rearrange("(p a) -> p a", a=1)

        def spread_row(a, parts):
            return a.rearrange("(a n) -> a n", a=1).broadcast_to([parts, a.shape[0]])

        def finish_softmax():
            with nc.cleanup_on_exit(), ExitStack() as ctx:
                big = sb("big", [P, NB * P], F32, ctx)
                ut = sb("ut", [P, N], F32, ctx)
                G = big[0:NP, :].rearrange("p (b f) -> p b f", b=NB)
                Y = big[:, 0:N]
                small = sb("small2", [NP, 4, NB], F32, ctx)
                w_a = sb("w_a", [D, H], F32, ctx)
                w_b = sb("w_b", [H, D], F32, ctx)
                cols = sb("cols", [H, 8], F32, ctx)
                b2row = sb("b2row", [NP, D], F32, ctx)
                scale_c = sb("scale_c", [NP, 1], F32, ctx)
                eps_h = sb("eps_h", [H, 1], F32, ctx)
                ps_t = ctx.enter_context(nc.psum_tensor("n0_ps_t", [D, 2, 512], F32))
                ps_y = ctx.enter_context(nc.psum_tensor("n0_ps_y", [H, 2, 512], F32))
                ps_z = ctx.enter_context(nc.psum_tensor("n0_ps_z", [NP, 2, 512], F32))
                got_w, gathered, ran, sq_ready, rooted, u_ready, turned, moved, hidden, biased, mean_ready, var_done, \
                    std_in, std_out, scaled, relued, z_ready, z_taken, var_ready, std_ready, normed, put, a_step = counter(
                        "n0_got_w n0_gathered n0_ran n0_sq n0_rooted n0_u n0_turned n0_moved n0_hidden n0_biased n0_mean "
                        "n0_var n0_std_in n0_std_out n0_scaled n0_relued n0_z n0_ztaken n0_var_ready n0_std_ready "
                        "n0_normed n0_put n0_astep", ctx)
                COLS = GROUP * NP
                ZG = 8
                zgroups = [(z, min(z + ZG, NB)) for z in range(0, NB, ZG)]
                with nc.Block() as block:
                    @block.sync
                    def _(sp):
                        sp.dma_start(w_a[:, :], w0a).then_inc(got_w, 16)
                        sp.dma_start(w_b[:, :], w0b).then_inc(got_w, 16)
                        for j, a in enumerate((b0a, gamma, beta)):
                            sp.dma_start(cols[:, j:j + 1], col(a)).then_inc(got_w, 16)
                        sp.dma_start(b2row[:, :], spread_row(b0b, NP)).then_inc(got_w, 16)
                        sp.dma_start(scale_c[:, :], spread_row(scale0, NP)).then_inc(got_w, 16)
                        sp.wait_ge(normed, 1)
                        sp.dma_start(nodes(table1), Hn[:, :, :]).then_inc(put, 16)
                        sp.wait_ge(put, 16)

                    @block.gpsimd
                    def _(pool):
                        gather_last(pool, G, scan0, gathered)
                        pool.wait_ge(gathered, 16 * NB)

                    @block.vector
                    def _(dve):
                        v = nc.vector
                        step = stepper(dve, ran)
                        m2, f2, inv = small[:, 0, :], small[:, 1, :], small[:, 2, :]
                        step(v.memset(eps_h[:, :], 1e-5))
                        step(v.tensor_tensor(T[:, :, :], Hn[:, :, :], Hn[:, :, :], ALU.mult))
                        step(v.reduce_sum(f2, T[:, :, :], AX))
                        dve.wait_ge(gathered, 16 * NB)
                        step(v.reciprocal(G[:, :, 0:D], G[:, :, 0:D]))
                        step(v.tensor_tensor(G[:, :, D:P], G[:, :, D:P], G[:, :, 0:D], ALU.mult))
                        step(v.tensor_tensor(G[:, :, D:P], G[:, :, D:P], bc(has_edge[:, :]), ALU.mult))
                        step(v.tensor_tensor(T[:, :, :], G[:, :, D:P], G[:, :, D:P], ALU.mult))
                        step(v.reduce_sum(m2, T[:, :, :], AX))
                        dve.sem_inc(sq_ready, 1)
                        dve.wait_ge(rooted, 1)
                        dve.wait_ge(got_w, 16 * 7)
                        step(v.tensor_scalar(m2, m2, 1e-12, None, ALU.max))
                        step(v.reciprocal(inv, m2))
                        step(v.tensor_tensor(inv, inv, f2, ALU.mult))
                        step(v.tensor_scalar(inv, inv, scale_c[:, :], None, ALU.mult))
                        step(v.tensor_tensor(T[:, :, :], G[:, :, D:P], bc(inv), ALU.mult))
                        step(v.tensor_tensor(T[:, :, :], T[:, :, :], Hn[:, :, :], ALU.add))
                        dve.sem_inc(u_ready, 1)
                        step(v.tensor_tensor(X[:, :, :], X[:, :, :], b2row[:, None, :].broadcast_to([NP, NB, D]), ALU.add))
                        dve.wait_ge(biased, GROUPS)
                        mean, var, mult, shift = (cols[:, j:j + 1] for j in range(3, 7))
                        step(v.reduce_sum(mean, Y, AX))
                        step(v.tensor_scalar(mean, mean, -1.0 / N, None, ALU.mult))
                        dve.sem_inc(mean_ready, 1)
                        dve.wait_ge(std_out, 1)
                        step(v.reciprocal(mult, var))
                        step(v.tensor_tensor(mult, mult, cols[:, 1:2], ALU.mult))
                        step(v.tensor_tensor(shift, mean, mult, ALU.mult))
                        step(v.tensor_tensor(shift, shift, cols[:, 2:3], ALU.add))
                        dve.sem_inc(scaled, 1)
                        for g, (z0, z1) in enumerate(zgroups):
                            dve.wait_ge(z_ready, g + 1)
                            v.tensor_tensor(X[:, z0:z1, :], X[:, z0:z1, :],
                                            ps_z[:, g % 2, 0:(z1 - z0) * D].rearrange("p (b f) -> p b f", f=D), ALU.add) \
                                .then_inc(z_taken, 1)
                        dve.wait_ge(z_taken, len(zgroups))
                        layernorm_relu(dve, step, small, X, Hn, var_ready, std_ready)
                        dve.sem_inc(normed, 1)

                    @block.tensor
                    def _(pe):
                        pe.wait_ge(u_ready, 1)
                        pe.wait_ge(got_w, 16 * 7)
                        for g in range(GROUPS + 1):
                            if g < GROUPS:
                                if g >= 2:
                                    pe.wait_ge(moved, g - 1)
                                for k in range(GROUP):
                                    mm = nc.tensor.transpose(ps_t[:, g % 2, k * NP:(k + 1) * NP], T[:, g * GROUP + k, :],
                                                             ident[0:NP, 0:NP])
                                mm.then_inc(turned, 1)
                            if g >= 1:
                                h = g - 1
                                pe.wait_ge(moved, h + 1)
                                if h >= 2:
                                    pe.wait_ge(biased, h - 1)
                                nc.tensor.matmul(ps_y[:, h % 2, 0:COLS], w_a[:, :], ut[0:D, h * COLS:(h + 1) * COLS],
                                                 start=True, stop=True).then_inc(hidden, 1)
                        pe.wait_ge(relued, 1)
                        for g, (z0, z1) in enumerate(zgroups):
                            if g >= 2:
                                pe.wait_ge(z_taken, g - 1)
                            for z in range(z0, z1):
                                mm = nc.tensor.matmul(ps_z[:, g % 2, (z - z0) * D:(z - z0 + 1) * D],
                                                      Y[:, z * NP:(z + 1) * NP], w_b[:, :], start=True, stop=True)
                            mm.then_inc(z_ready, 1)

                    @block.scalar
                    def _(act):
                        a = nc.scalar
                        act.wait_ge(sq_ready, 1)
                        a.activation(small[:, 0:2, :], small[:, 0:2, :], ACT.Sqrt).then_inc(rooted, 1)
                        for g in range(GROUPS + 1):
                            if g < GROUPS:
                                act.wait_ge(turned, g + 1)
                                a.activation(ut[0:D, g * COLS:(g + 1) * COLS], ps_t[:, g % 2, 0:COLS], ACT.Copy).then_inc(moved, 1)
                            if g >= 1:
                                h = g - 1
                                act.wait_ge(hidden, h + 1)
                                a.activation(Y[:, h * COLS:(h + 1) * COLS], ps_y[:, h % 2, 0:COLS], ACT.Identity,
                                             bias=cols[:, 0:1]).then_inc(biased, 1)
                        act.wait_ge(mean_ready, 1)
                        a.activation(ut[:, :], Y, ACT.Square, bias=cols[:, 3:4], accum_out=cols[:, 4:5]).then_inc(var_done, 1)
                        act.wait_ge(var_done, 1)
                        a.activation(cols[:, 4:5], cols[:, 4:5], ACT.Sqrt, bias=eps_h[:, :], scale=1.0 / N).then_inc(std_out, 1)
                        act.wait_ge(scaled, 1)
                        a.activation(Y, Y, ACT.Relu, bias=cols[:, 6:7], scale=cols[:, 5:6]).then_inc(relued, 1)
                        layernorm_std(act, small, eps5[:, :], var_ready, std_ready)

        c_cols = sb("c_cols", [P, 8], F32)

        def atanh_over(dve, step, sem_in, sem_out, k, y, norm, s, out_f):
            v = nc.vector
            yc, l1, l2, q = (s[:, j, :] for j in range(4))
            step(v.tensor_scalar(yc, y, -0.9, 0.9, ALU.max, ALU.min))
            dve.sem_inc(sem_in, 1)
            step(v.tensor_tensor(q, yc, yc, ALU.mult))
            step(v.tensor_scalar(out_f, q, 1.0 / 11, 1.0 / 9, ALU.mult, ALU.add))
            for n in (7, 5, 3, 1):
                step(v.tensor_tensor(out_f, out_f, q, ALU.mult))
                step(v.tensor_scalar(out_f, out_f, 1.0 / n, None, ALU.add))
            step(v.tensor_tensor(out_f, out_f, yc, ALU.mult))
            dve.wait_ge(sem_out, k)
            step(v.tensor_tensor(l1, l1, l2, ALU.subtract))
            step(v.tensor_scalar(l1, l1, 0.5, None, ALU.mult))
            step(v.tensor_scalar(q, q, 0.03, None, ALU.is_lt))
            step(v.tensor_tensor(out_f, out_f, l1, ALU.subtract))
            step(v.tensor_tensor(out_f, out_f, q, ALU.mult))
            step(v.tensor_tensor(out_f, out_f, l1, ALU.add))
            step(v.reciprocal(l2, norm))
            step(v.tensor_tensor(out_f, out_f, l2, ALU.mult))

        def logarithms(act, sem_in, sem_out, k, s):
            act.wait_ge(sem_in, k)
            nc.scalar.activation(s[:, 1, :], s[:, 0, :], ACT.Ln, bias=1.0)
            nc.scalar.activation(s[:, 2, :], s[:, 0, :], ACT.Ln, bias=1.0, scale=-1.0).then_inc(sem_out, 1)

        def norms(dve, step, src_rows, out_n, sem_in, sem_out, k):
            step(nc.vector.tensor_tensor(T[:, :, :], src_rows, src_rows, ALU.mult))
            step(nc.vector.reduce_sum(out_n, T[:, :, :], AX))
            dve.sem_inc(sem_in, 1)
            dve.wait_ge(sem_out, k)

        def clip_norm(step, norm, limit, factor_out, tmp):
            v = nc.vector
            step(v.tensor_scalar(tmp, norm, limit, None, ALU.max))
            step(v.reciprocal(factor_out, tmp))
            step(v.tensor_scalar(factor_out, factor_out, limit, None, ALU.mult))
            step(v.tensor_tensor(norm, norm, factor_out, ALU.mult))

        def finish_mean():
            with nc.cleanup_on_exit(), ExitStack() as ctx:
                G = sb("G1", [NP, NB, 2 * D], F32, ctx)
                w_rows = sb("w1_rows", [D, 2 * D], F32, ctx)
                w_t = sb("w1_t", [2 * D, D], F32, ctx)
                w_p = sb("w2_s", [D, D], F32, ctx)
                b_row = sb("b1_row", [NP, D], F32, ctx)
                s = sb("s1", [NP, 12, NB], F32, ctx)
                table = sb("table2_s", [NP, NB, ROW2], F32, ctx)
                ps_w = ctx.enter_context(nc.psum_tensor("n1_ps_w", [2 * D, 512], F32))
                lin1 = Linear(ctx, "lin1", 2 * D, D)
                lin2 = Linear(ctx, "lin2", D, D, banks_of=lin1)
                got_w, gathered, ran, agg_ready, w_turned, w_moved, var_ready, std_ready, ask_root, root, ask_tanh, \
                    tanhed, ask_log, logged, p_ready, put, tabled, c_ready, c_root = counter(
                        "n1_got_w n1_gathered n1_ran n1_agg n1_wturned n1_wmoved n1_var_ready n1_std_ready n1_ask_root "
                        "n1_root n1_ask_tanh n1_tanhed n1_ask_log n1_logged n1_p n1_put n1_tabled n1_cready n1_croot", ctx)
                nf, s1, tmp, th, np_, s2, k1, tn = (s[:, j, :] for j in range(4, 12))
                with nc.Block() as block:
                    @block.sync
                    def _(sp):
                        sp.dma_start(w_rows[:, :], w1).then_inc(got_w, 16)
                        sp.dma_start(w_p[:, :], w2).then_inc(got_w, 16)
                        sp.dma_start(b_row[:, :], spread_row(b1, NP)).then_inc(got_w, 16)
                        sp.dma_start(c_cols[:, 0:1], spread_row(c2, P)).then_inc(got_w, 16)
                        sp.wait_ge(tabled, 1)
                        sp.dma_start(nodes(table2), table[:, :, :]).then_inc(put, 16)
                        sp.wait_ge(put, 16)

                    @block.gpsimd
                    def _(pool):
                        gather_last(pool, table[:, :, 0:D], scan1, gathered)
                        pool.wait_ge(gathered, 16 * NB)

                    @block.tensor
                    def _(pe):
                        pe.wait_ge(got_w, 64)
                        nc.tensor.transpose(ps_w[:, 0:D], w_rows[:, :], ident[0:D, 0:D]).then_inc(w_turned, 1)
                        pe.wait_ge(w_moved, 1)
                        pe.wait_ge(agg_ready, 1)
                        lin1.pe(pe, G, w_t[:, :])
                        pe.wait_ge(p_ready, 1)
                        lin2.pe(pe, G[:, :, 0:D], w_p[:, :])

                    @block.scalar
                    def _(act):
                        a = nc.scalar
                        act.wait_ge(w_turned, 1)
                        a.activation(w_t[:, :], ps_w[:, 0:D], ACT.Copy).then_inc(w_moved, 1)
                        act.wait_ge(got_w, 64)
                        a.activation(c_cols[:, 1:2], c_cols[:, 0:1], ACT.Sqrt).then_inc(c_root, 1)
                        lin1.act(act)
                        layernorm_std(act, s, eps5[:, :], var_ready, std_ready)

                        def roots(k, tile):
                            act.wait_ge(ask_root, k)
                            a.activation(tile, tile, ACT.Sqrt).then_inc(root, 1)

                        def tanhs(k, to, of):
                            act.wait_ge(ask_tanh, k)
                            a.activation(to, of, ACT.Tanh).then_inc(tanhed, 1)
                        roots(1, nf)
                        tanhs(1, th, nf)
                        roots(2, np_)
                        logarithms(act, ask_log, logged, 1, s)
                        lin2.act(act)
                        roots(3, tn)
                        tanhs(2, th, tmp)
                        roots(4, nf)
                        logarithms(act, ask_log, logged, 2, s)

                    @block.vector
                    def _(dve):
                        v = nc.vector
                        step = stepper(dve, ran)
                        c, sc, isc, clip_c = (c_cols[:, j:j + 1] for j in range(4))
                        c_, sc_, isc_, clip_c_ = (c_cols[0:NP, j:j + 1] for j in range(4))
                        dve.wait_ge(c_root, 1)
                        step(v.reciprocal(isc, sc))
                        step(v.tensor_scalar(clip_c, isc, CLIP, None, ALU.mult))
                        step(v.tensor_copy(G[:, :, D:2 * D], Hn[:, :, :]))
                        step(v.tensor_tensor(s[:, 0, :], inv_deg[:, :], has_edge[:, :], ALU.mult))
                        step(v.tensor_tensor(X[:, :, :], X[:, :, :], b_row[:, None, :].broadcast_to([NP, NB, D]), ALU.add))
                        dve.wait_ge(gathered, 16 * NB)
                        step(v.tensor_tensor(G[:, :, 0:D], table[:, :, 0:D], bc(s[:, 0, :]), ALU.mult))
                        dve.sem_inc(agg_ready, 1)
                        lin1.take(dve, lambda g, y: v.tensor_tensor(
                            X[:, g * GROUP:(g + 1) * GROUP, :], X[:, g * GROUP:(g + 1) * GROUP, :],
                            y[:, 0, 0:GROUP * D].rearrange("p (b f) -> p b f", f=D), ALU.add))
                        dve.wait_ge(lin1.taken, lin1.n)
                        layernorm_relu(dve, step, s, X, Hn, var_ready, std_ready)

                        p = G[:, :, 0:D]
                        step(v.tensor_scalar(p, Hn[:, :, :], EPS2, None, ALU.add))
                        norms(dve, step, p, nf, ask_root, root, 1)
                        clip_norm(step, nf, CLIP, s1, tmp)
                        dve.sem_inc(ask_tanh, 1)
                        step(v.reciprocal(tmp, nf))
                        step(v.tensor_tensor(s1, s1, tmp, ALU.mult))
                        dve.wait_ge(tanhed, 1)
                        step(v.tensor_tensor(s1, s1, th, ALU.mult))
                        step(v.tensor_tensor(p, p, bc(s1), ALU.mult))
                        step(v.tensor_scalar(p, p, EPS2, None, ALU.add))
                        norms(dve, step, p, np_, ask_root, root, 2)
                        clip_norm(step, np_, CLIP, s2, tmp)
                        step(v.tensor_tensor(p, p, bc(s2), ALU.mult))
                        dve.sem_inc(p_ready, 1)
                        step(v.tensor_scalar(tmp, np_, sc_, None, ALU.mult))
                        atanh_over(dve, step, ask_log, logged, 1, tmp, np_, s, k1)
                        step(v.tensor_scalar(k1, k1, isc_, None, ALU.mult))
                        q = table[:, :, 0:D]
                        lin2.take(dve, lambda g, y: v.tensor_copy(
                            q[:, g * GROUP:(g + 1) * GROUP, :], y[:, 0, 0:GROUP * D].rearrange("p (b f) -> p b f", f=D)))
                        dve.wait_ge(lin2.taken, lin2.n)
                        step(v.tensor_tensor(q, q, bc(k1), ALU.mult))
                        norms(dve, step, q, tn, ask_root, root, 3)
                        clip_norm(step, tn, clip_c_, s1, tmp)
                        step(v.tensor_scalar(tmp, tn, sc_, None, ALU.mult))
                        dve.sem_inc(ask_tanh, 1)
                        step(v.reciprocal(s2, tmp))
                        step(v.tensor_tensor(s1, s1, s2, ALU.mult))
                        dve.wait_ge(tanhed, 2)
                        step(v.tensor_tensor(s1, s1, th, ALU.mult))
                        step(v.tensor_tensor(q, q, bc(s1), ALU.mult))
                        step(v.tensor_tensor(T[:, :, :], q, q, ALU.mult))
                        step(v.reduce_sum(s1, T[:, :, :], AX))
                        step(v.tensor_scalar(s1, s1, c_, None, ALU.mult))
                        step(v.tensor_scalar(table[:, :, D], s1, -1.0, 1.0, ALU.mult, ALU.add))
                        g = G[:, :, D:2 * D]
                        step(v.tensor_scalar(g, q, EPS2, None, ALU.add))
                        norms(dve, step, g, nf, ask_root, root, 4)
                        clip_norm(step, nf, CLIP, s1, tmp)
                        step(v.tensor_scalar(tmp, nf, sc_, None, ALU.mult))
                        atanh_over(dve, step, ask_log, logged, 2, tmp, nf, s, k1)
                        step(v.tensor_tensor(s1, s1, k1, ALU.mult))
                        step(v.tensor_scalar(table[:, :, D + 1], s1, sc_, None, ALU.mult))
                        dve.sem_inc(tabled, 1)

        def finish_hyperbolic():
            with nc.cleanup_on_exit(), ExitStack() as ctx:
                acc = sb("acc_s", [NP, 2, NB, ACC2], F32, ctx)
                w_all = sb("w3_all", [D, RELS, ROW3], F32, ctx)
                al = sb("al", [D, RELS * HEADS * DH], F32, ctx)
                ar = sb("ar", [D, RELS * HEADS * DH], F32, ctx)
                wa = sb("wa", [D, RELS, HEADS * DH], F32, ctx)
                s = sb("s2s", [NP, 12, NB], F32, ctx)
                rows_o = sb("rows_o", [NP, 2, RELS, SRC3], F32, ctx)
                dst_o = sb("dst_o", [NP, 2, RELS, HEADS], F32, ctx)
                lin3 = Linear(ctx, "lin3", D, RELS * ROW3)
                got_w, got_acc, ran, var_ready, std_ready, ask_root, root, ask_tanh, tanhed, ask_exp, exped, h_ready, \
                    put0, put1, slot_added = counter(
                        "n2_got_w n2_got_acc n2_ran n2_var_ready n2_std_ready n2_ask_root n2_root n2_ask_tanh n2_tanhed "
                        "n2_ask_exp n2_exped n2_h n2_put0 n2_put1 n2_slot_added", ctx)
                put = [put0, put1]
                den, fac, tmp, zn, th, nf = (s[:, j, :] for j in range(4, 10))
                with nc.Block() as block:
                    @block.sync
                    def _(sp):
                        for k in range(2):
                            sp.dma_start(acc[:, k, :, :], nodes(acc2[k])).then_inc(got_acc, 16)
                        for r in range(RELS):
                            sp.dma_start(w_all[:, r, 0:D].rearrange("p (h d) -> p h d", h=HEADS),
                                         w3[r].rearrange("h i d -> i h d")).then_inc(got_w, 16)
                        for t, a in ((al, al3), (ar, ar3)):
                            sp.dma_start(t[:, :], spread_row(a.rearrange("r h d -> (r h d)"), D)).then_inc(got_w, 16)
                        for k in range(2, TILES):
                            sp.wait_ge(got_acc, 16 * k)
                            sp.wait_ge(slot_added, k - 1)
                            sp.dma_start(acc[:, 1, :, :], nodes(acc2[k])).then_inc(got_acc, 16)
                        t3s = table3s.rearrange("(p b r) f -> p b (r f)", p=NP, b=NB)
                        t3d = table3d.rearrange("(p b r) f -> p b (r f)", p=NP, b=NB)
                        for g in range(NB):
                            sp.wait_ge(lin3.taken, g + 1)
                            sp.dma_start(t3s[:, g, :], rows_o[:, g % 2, :, :].rearrange("p r f -> p (r f)")).then_inc(put[g % 2], 16)
                            sp.dma_start(t3d[:, g, :], dst_o[:, g % 2, :, :].rearrange("p r f -> p (r f)")).then_inc(put[g % 2], 16)
                        for b in range(2):
                            sp.wait_ge(put[b], 16 * NB)

                    @block.tensor
                    def _(pe):
                        pe.wait_ge(h_ready, 1)
                        lin3.pe(pe, Hn, w_all[:, :, :].rearrange("p r f -> p (r f)"))

                    @block.scalar
                    def _(act):
                        a = nc.scalar
                        act.wait_ge(ask_exp, 1)
                        a.activation(T[:, :, :], T[:, :, :], ACT.Exp).then_inc(exped, 1)
                        act.wait_ge(ask_root, 1)
                        a.activation(zn, zn, ACT.Sqrt).then_inc(root, 1)
                        act.wait_ge(ask_tanh, 1)
                        a.activation(th, tmp, ACT.Tanh).then_inc(tanhed, 1)
                        layernorm_std(act, s, eps5[:, :], var_ready, std_ready)
                        lin3.act(act)

                    @block.vector
                    def _(dve):
                        v = nc.vector
                        step = stepper(dve, ran)
                        c_, sc_, isc_, clip_c_ = (c_cols[0:NP, j:j + 1] for j in range(4))
                        A, z = acc[:, 0, :, :], Hn[:, :, :]
                        dve.wait_ge(got_acc, 32)
                        step(v.tensor_tensor(A, A, acc[:, 1, :, :], ALU.add))
                        dve.sem_inc(slot_added, 1)
                        dve.wait_ge(got_acc, 48)
                        step(v.tensor_tensor(A, A, acc[:, 1, :, :], ALU.add))
                        dve.sem_inc(slot_added, 1)
                        dve.wait_ge(got_acc, 64)
                        step(v.tensor_tensor(A, A, acc[:, 1, :, :], ALU.add))
                        step(v.tensor_scalar(den, A[:, :, D], 1e-16, None, ALU.add))
                        step(v.reciprocal(fac, den))
                        step(v.tensor_tensor(z, A[:, :, 0:D], bc(fac), ALU.mult))
                        step(v.tensor_scalar(T[:, :, :], z, 0.0, None, ALU.min))
                        dve.sem_inc(ask_exp, 1)
                        step(v.tensor_scalar(z, z, 0.0, None, ALU.max))
                        dve.wait_ge(exped, 1)
                        step(v.scalar_tensor_tensor(z, T[:, :, :], -1.0, z, ALU.add, ALU.add))
                        step(v.tensor_scalar(z, z, EPS2, None, ALU.add))
                        norms(dve, step, z, zn, ask_root, root, 1)
                        clip_norm(step, zn, clip_c_, fac, tmp)
                        step(v.tensor_scalar(tmp, zn, sc_, None, ALU.mult))
                        dve.sem_inc(ask_tanh, 1)
                        step(v.reciprocal(nf, tmp))
                        step(v.tensor_tensor(fac, fac, nf, ALU.mult))
                        dve.wait_ge(tanhed, 1)
                        step(v.tensor_tensor(fac, fac, th, ALU.mult))
                        step(v.tensor_tensor(z, z, bc(fac), ALU.mult))
                        step(v.tensor_tensor(X[:, :, :], X[:, :, :], z, ALU.add))
                        layernorm_relu(dve, step, s, X, Hn, var_ready, std_ready)
                        dve.wait_ge(got_w, 16 * (RELS + 2))
                        for t, at in ((al, D), (ar, D + HEADS)):
                            step(v.tensor_tensor(wa[:, :, :], w_all[:, :, 0:D], t[:, :].rearrange("p (r f) -> p r f", r=RELS), ALU.mult))
                            step(v.reduce_sum(w_all[:, :, at:at + HEADS], wa[:, :, :].rearrange("p r (h d) -> p r h d", h=HEADS), AX))
                        dve.sem_inc(h_ready, 1)

                        def take(g, y):
                            if g >= 2:
                                dve.wait_ge(put[g % 2], 32 * (g // 2))
                            both = y[:, :, 0:RELS * ROW3 // 2].rearrange("p t (r f) -> p t r f", f=ROW3)
                            step(v.tensor_copy(rows_o[:, g % 2, :, :].rearrange("p (t r) f -> p t r f", t=2), both[:, :, :, 0:SRC3]))
                            return v.tensor_copy(dst_o[:, g % 2, :, :].rearrange("p (t r) f -> p t r f", t=2), both[:, :, :, SRC3:ROW3])
                        lin3.take(dve, take)

        def finish_relational():
            with nc.cleanup_on_exit(), ExitStack() as ctx:
                G = sb("G3", [NP, NB, 2 * D], F32, ctx)
                b_row = sb("b3_row", [NP, D], F32, ctx)
                got_w, gathered, ran, done, put = counter("n3_got_w n3_gathered n3_ran n3_done n3_put", ctx)
                with nc.Block() as block:
                    @block.sync
                    def _(sp):
                        sp.dma_start(b_row[:, :], spread_row(b3, NP)).then_inc(got_w, 16)
                        sp.wait_ge(done, 1)
                        sp.dma_start(nodes(out), X[:, :, :]).then_inc(put, 16)
                        sp.wait_ge(put, 16)

                    @block.gpsimd
                    def _(pool):
                        gather_last(pool, G, scan3, gathered)
                        pool.wait_ge(gathered, 16 * NB)

                    @block.vector
                    def _(dve):
                        v = nc.vector
                        step = stepper(dve, ran)
                        dve.wait_ge(got_w, 16)
                        step(v.tensor_tensor(X[:, :, :], X[:, :, :], b_row[:, None, :].broadcast_to([NP, NB, D]), ALU.add))
                        dve.wait_ge(gathered, 16 * NB)
                        step(v.tensor_scalar(G[:, :, 0:D], G[:, :, 0:D], 1e-16, None, ALU.max))
                        step(v.reciprocal(G[:, :, 0:D], G[:, :, 0:D]))
                        step(v.tensor_tensor(G[:, :, D:2 * D], G[:, :, D:2 * D], G[:, :, 0:D], ALU.mult))
                        step(v.tensor_tensor(G[:, :, D:2 * D], G[:, :, D:2 * D], bc(has_edge[:, :]), ALU.mult))
                        step(v.tensor_tensor(X[:, :, :], X[:, :, :], G[:, :, D:2 * D], ALU.add))
                        dve.sem_inc(done, 1)

        softmax_edges(0)
        finish_softmax()
        mean_edges()
        finish_mean()
        hyperbolic_edges(c_cols[:, 0:1], c_cols[:, 2:3])
        finish_hyperbolic()
        softmax_edges(3)
        finish_relational()


_INS = ["x", "src", "dst", "edge_attr_64", "edge_type_8", "L0_gnn_W1", "L0_gnn_b1", "L0_gnn_gamma", "L0_gnn_bn_beta",
        "L0_gnn_W2", "L0_gnn_b2", "L0_gnn_scale", "L1_gnn_W", "L1_gnn_b", "L2_gnn_W", "L2_gnn_c",
        "L3_gnn_conv_weights", "L3_gnn_attn_l", "L3_gnn_attn_r", "L3_gnn_h_bias"]


def kernel(**inputs):
    import numpy as np
    import concourse.bacc as bacc
    from concourse.bass_utils import run_bass_kernel_spmd as run

    nc = bacc.Bacc("TRN2", target_bir_lowering=False, num_devices=1)
    arrays, args = {}, []
    for name in _INS:
        a = np.ascontiguousarray(inputs[name])
        arrays[f"in_{name}"] = a
        args.append(nc.dram_tensor(f"in_{name}", a.shape, mybir.dt.from_np(a.dtype), kind="ExternalInput").ap())
    args.append(nc.dram_tensor("out_0", (N, D), F32, kind="ExternalOutput").ap())
    build(nc, *args)
    r = run(nc, [arrays], core_ids=[0])
    return r.results[0]["out_0"]
```
